# Optimizing a Trainium2 kernel written in Bass

```python
import numpy as np
import jax
import jax.numpy as jnp

def _softmax(x, axis=-1):
    return jax.nn.softmax(x, axis=axis)

def _gelu(x):
    return jax.nn.gelu(x, approximate=True)

def _silu(x):
    return jax.nn.silu(x)

def _sigmoid(x):
    return jax.nn.sigmoid(x)

def _layernorm(x, axis=-1, eps=1e-05):
    m = jnp.mean(x, axis=axis, keepdims=True)
    v = jnp.var(x, axis=axis, keepdims=True)
    return (x - m) / jnp.sqrt(v + eps)

def _scatter_add(tgt, idx, src, axis=0):
    return tgt.at[idx].add(src)

def _segment_sum(src, seg, n):
    return jax.ops.segment_sum(src, seg, n)
kernel_name = 'mk_sandwich_d1_jaxref_r4_b998a3'

def setup_inputs(seed: int=0):
    np.random.seed(seed)
    _w = jnp.asarray

    def _L0_attn_setup():
        import jax, jax.numpy as jnp
        import numpy as np
        B, S, DM, DI, H = (2, 512, 256, 512, 32)
        HD = DI // H
        G = 32

        def _forward(x, in_proj_W, in_proj_b, conv_w, conv_b, dyn_W, dyn_b, dt_c, selB_W, selC_W, seldt_W, beta_W, beta_b, rg_W, rg_b, ug_W, ug_b, Q_W, out_W, D, rms_w, gn_w, gn_b):
            b, s, _ = x.shape
            residual = x
            xn = x * jax.lax.rsqrt(jnp.mean(x * x, -1, keepdims=True) + 1e-06) * rms_w
            proj = xn @ in_proj_W.T + in_proj_b
            z = proj[..., :DI]
            K = proj[..., DI:3 * DI].reshape(b, s, DI, 2)
            V = proj[..., 3 * DI:]
            vc = jax.lax.conv_general_dilated(V.transpose(0, 2, 1), conv_w[:, None, :], (1,), [(3, 0)], feature_group_count=DI, dimension_numbers=('NCH', 'OIH', 'NCH'))
            u = jax.nn.silu(vc + conv_b[None, :, None]).transpose(0, 2, 1)
            dyn = u @ dyn_W.T + dyn_b
            alpha = jax.nn.softplus(dyn[..., :H])
            omega = dyn[..., H:2 * H] + dyn[..., 2 * H:3 * H]
            rope = 1.0 / 10000.0 ** (jnp.arange(H, dtype=jnp.float32) / H)
            omega = omega + jnp.arange(s, dtype=jnp.float32)[None, :, None] * rope
            dt = jax.nn.softplus(dt_c) / (alpha + jnp.abs(omega) + 0.0001)
            dt = dt + jax.nn.softplus(u @ seldt_W.T)
            sel_B = (u @ selB_W.T).reshape(b, s, H, 1, 2)
            sel_C = (u @ selC_W.T).reshape(b, s, H, 1, 2)
            Kh = K.reshape(b, s, H, HD, 2) * sel_B
            a = 0.5 * dt * alpha
            w = 0.5 * dt * omega
            det = (1.0 + a) ** 2 + w * w
            lam2 = ((1.0 - a) ** 2 + w * w) / det
            r_gate = jax.nn.sigmoid(u @ rg_W.T + rg_b)
            vp = jnp.sqrt(jnp.clip(1.0 - lam2 ** r_gate, 1e-06))
            u_gate = jax.nn.sigmoid(u @ ug_W.T + ug_b)
            Vg = u.reshape(b, s, H, HD) * (vp * u_gate)[..., None]
            Q = (u @ Q_W.T).reshape(b, s, H, HD, 2) * sel_C
            beta = jax.nn.sigmoid(u @ beta_W.T + beta_b)
            A11 = (1.0 - a * a - w * w) / det
            A12 = 2.0 * w / det

            def step(Sc, inp):
                a11, a12, bt, k, v = inp
                S0, S1 = (Sc[..., 0], Sc[..., 1])
                r0 = a11[..., None] * S0 + a12[..., None] * S1
                r1 = -a12[..., None] * S0 + a11[..., None] * S1
                Sr = jnp.stack([r0, r1], -1)
                err = v - jnp.sum(k * Sr, -1)
                Sn = Sr + bt[..., None, None] * err[..., None] * k
                return (Sn, Sn)
            xs = (jnp.swapaxes(A11, 0, 1), jnp.swapaxes(A12, 0, 1), jnp.swapaxes(beta, 0, 1), jnp.swapaxes(Kh, 0, 1), jnp.swapaxes(Vg, 0, 1))
            S0 = jnp.zeros((b, H, HD, 2), x.dtype)
            _, Y = jax.lax.scan(step, S0, xs)
            Y = jnp.moveaxis(Y, 0, 1)
            y = jnp.sum(Q * Y, -1).reshape(b, s, DI)
            yg = y.transpose(0, 2, 1).reshape(b, G, DI // G, s)
            mu = jnp.mean(yg, (2, 3), keepdims=True)
            var = jnp.var(yg, (2, 3), keepdims=True)
            yg = (yg - mu) * jax.lax.rsqrt(var + 1e-05)
            y = (yg.reshape(b, DI, s) * gn_w[None, :, None] + gn_b[None, :, None]).transpose(0, 2, 1)
            y = y * jax.nn.silu(z)
            y = y + D * u
            return residual + y @ out_W.T
        key = jax.random.key(seed)
        ks = list(jax.random.split(key, 12))
        r = lambda k, shp, std: jax.random.normal(k, shp, jnp.float32) * std
        sel_std = 1.0 / float(np.sqrt(DI))
        return dict(x=jax.random.normal(ks[0], (B, S, DM), jnp.float32), in_proj_W=r(ks[1], (4 * DI, DM), 0.02), in_proj_b=jnp.zeros((4 * DI,), jnp.float32), conv_w=r(ks[2], (DI, 4), 0.3), conv_b=jnp.zeros((DI,), jnp.float32), dyn_W=r(ks[3], (3 * H, DI), 0.02), dyn_b=jnp.zeros((3 * H,), jnp.float32), dt_c=jnp.full((H,), 0.5, jnp.float32), selB_W=r(ks[4], (2 * H, DI), sel_std), selC_W=r(ks[5], (2 * H, DI), sel_std), seldt_W=r(ks[6], (H, DI), sel_std), beta_W=r(ks[7], (H, DI), sel_std), beta_b=jnp.zeros((H,), jnp.float32), rg_W=r(ks[8], (H, DI), sel_std), rg_b=jnp.ones((H,), jnp.float32), ug_W=r(ks[9], (H, DI), sel_std), ug_b=jnp.full((H,), -1.0, jnp.float32), Q_W=jnp.repeat(jnp.eye(DI, dtype=jnp.float32), 2, axis=0), out_W=r(ks[10], (DM, DI), 0.02), D=jnp.zeros((DI,), jnp.float32), rms_w=jnp.ones((DM,), jnp.float32), gn_w=jnp.ones((DI,), jnp.float32), gn_b=jnp.zeros((DI,), jnp.float32))
    _L0_attn_in = _L0_attn_setup()

    def _L0_ffn_setup():
        import jax, jax.numpy as jnp
        import numpy as np
        B, T, D, F_FF, E, K = (8, 512, 256, 1024, 8, 2)
        key = jax.random.key(seed)
        ks = jax.random.split(key, 6)
        s = 1.0 / np.sqrt(D)
        return {'x': jax.random.normal(ks[0], (B, T, D), jnp.float32), 'Wr': jax.random.normal(ks[1], (D, E), jnp.float32) * s, 'W1': jax.random.normal(ks[2], (E, D, F_FF), jnp.float32) * s, 'b1': jax.random.normal(ks[3], (E, F_FF), jnp.float32) * 0.01, 'W2': jax.random.normal(ks[4], (E, F_FF, D), jnp.float32) * (1.0 / np.sqrt(F_FF)), 'b2': jax.random.normal(ks[5], (E, D), jnp.float32) * 0.01}
    _L0_ffn_in = _L0_ffn_setup()
    _d = {'L0_attn_x': _L0_attn_in['x'], 'L0_attn_in_proj_W': _L0_attn_in['in_proj_W'], 'L0_attn_in_proj_b': _L0_attn_in['in_proj_b'], 'L0_attn_conv_w': _L0_attn_in['conv_w'], 'L0_attn_conv_b': _L0_attn_in['conv_b'], 'L0_attn_dyn_W': _L0_attn_in['dyn_W'], 'L0_attn_dyn_b': _L0_attn_in['dyn_b'], 'L0_attn_dt_c': _L0_attn_in['dt_c'], 'L0_attn_selB_W': _L0_attn_in['selB_W'], 'L0_attn_selC_W': _L0_attn_in['selC_W'], 'L0_attn_seldt_W': _L0_attn_in['seldt_W'], 'L0_attn_beta_W': _L0_attn_in['beta_W'], 'L0_attn_beta_b': _L0_attn_in['beta_b'], 'L0_attn_rg_W': _L0_attn_in['rg_W'], 'L0_attn_rg_b': _L0_attn_in['rg_b'], 'L0_attn_ug_W': _L0_attn_in['ug_W'], 'L0_attn_ug_b': _L0_attn_in['ug_b'], 'L0_attn_Q_W': _L0_attn_in['Q_W'], 'L0_attn_out_W': _L0_attn_in['out_W'], 'L0_attn_D': _L0_attn_in['D'], 'L0_attn_rms_w': _L0_attn_in['rms_w'], 'L0_attn_gn_w': _L0_attn_in['gn_w'], 'L0_attn_gn_b': _L0_attn_in['gn_b'], 'L0_ffn_Wr': _L0_ffn_in['Wr'], 'L0_ffn_W1': _L0_ffn_in['W1'], 'L0_ffn_b1': _L0_ffn_in['b1'], 'L0_ffn_W2': _L0_ffn_in['W2'], 'L0_ffn_b2': _L0_ffn_in['b2']}
    _x0 = _d['L0_attn_x']
    _d['L0_attn_x'] = jax.random.normal(jax.random.fold_in(jax.random.key(seed), 1), (2, 2048, 256), dtype=_x0.dtype)
    del _x0
    return _d

def reference(L0_attn_x, L0_attn_in_proj_W, L0_attn_in_proj_b, L0_attn_conv_w, L0_attn_conv_b, L0_attn_dyn_W, L0_attn_dyn_b, L0_attn_dt_c, L0_attn_selB_W, L0_attn_selC_W, L0_attn_seldt_W, L0_attn_beta_W, L0_attn_beta_b, L0_attn_rg_W, L0_attn_rg_b, L0_attn_ug_W, L0_attn_ug_b, L0_attn_Q_W, L0_attn_out_W, L0_attn_D, L0_attn_rms_w, L0_attn_gn_w, L0_attn_gn_b, L0_ffn_Wr, L0_ffn_W1, L0_ffn_b1, L0_ffn_W2, L0_ffn_b2):

    def _L0_attn_ref(x, in_proj_W, in_proj_b, conv_w, conv_b, dyn_W, dyn_b, dt_c, selB_W, selC_W, seldt_W, beta_W, beta_b, rg_W, rg_b, ug_W, ug_b, Q_W, out_W, D, rms_w, gn_w, gn_b):
        import jax, jax.numpy as jnp
        import numpy as np
        B, S, DM, DI, H = (2, 512, 256, 512, 32)
        HD = DI // H
        G = 32

        def _forward(x, in_proj_W, in_proj_b, conv_w, conv_b, dyn_W, dyn_b, dt_c, selB_W, selC_W, seldt_W, beta_W, beta_b, rg_W, rg_b, ug_W, ug_b, Q_W, out_W, D, rms_w, gn_w, gn_b):
            b, s, _ = x.shape
            residual = x
            xn = x * jax.lax.rsqrt(jnp.mean(x * x, -1, keepdims=True) + 1e-06) * rms_w
            proj = xn @ in_proj_W.T + in_proj_b
            z = proj[..., :DI]
            K = proj[..., DI:3 * DI].reshape(b, s, DI, 2)
            V = proj[..., 3 * DI:]
            vc = jax.lax.conv_general_dilated(V.transpose(0, 2, 1), conv_w[:, None, :], (1,), [(3, 0)], feature_group_count=DI, dimension_numbers=('NCH', 'OIH', 'NCH'))
            u = jax.nn.silu(vc + conv_b[None, :, None]).transpose(0, 2, 1)
            dyn = u @ dyn_W.T + dyn_b
            alpha = jax.nn.softplus(dyn[..., :H])
            omega = dyn[..., H:2 * H] + dyn[..., 2 * H:3 * H]
            rope = 1.0 / 10000.0 ** (jnp.arange(H, dtype=jnp.float32) / H)
            omega = omega + jnp.arange(s, dtype=jnp.float32)[None, :, None] * rope
            dt = jax.nn.softplus(dt_c) / (alpha + jnp.abs(omega) + 0.0001)
            dt = dt + jax.nn.softplus(u @ seldt_W.T)
            sel_B = (u @ selB_W.T).reshape(b, s, H, 1, 2)
            sel_C = (u @ selC_W.T).reshape(b, s, H, 1, 2)
            Kh = K.reshape(b, s, H, HD, 2) * sel_B
            a = 0.5 * dt * alpha
            w = 0.5 * dt * omega
            det = (1.0 + a) ** 2 + w * w
            lam2 = ((1.0 - a) ** 2 + w * w) / det
            r_gate = jax.nn.sigmoid(u @ rg_W.T + rg_b)
            vp = jnp.sqrt(jnp.clip(1.0 - lam2 ** r_gate, 1e-06))
            u_gate = jax.nn.sigmoid(u @ ug_W.T + ug_b)
            Vg = u.reshape(b, s, H, HD) * (vp * u_gate)[..., None]
            Q = (u @ Q_W.T).reshape(b, s, H, HD, 2) * sel_C
            beta = jax.nn.sigmoid(u @ beta_W.T + beta_b)
            A11 = (1.0 - a * a - w * w) / det
            A12 = 2.0 * w / det

            def step(Sc, inp):
                a11, a12, bt, k, v = inp
                S0, S1 = (Sc[..., 0], Sc[..., 1])
                r0 = a11[..., None] * S0 + a12[..., None] * S1
                r1 = -a12[..., None] * S0 + a11[..., None] * S1
                Sr = jnp.stack([r0, r1], -1)
                err = v - jnp.sum(k * Sr, -1)
                Sn = Sr + bt[..., None, None] * err[..., None] * k
                return (Sn, Sn)
            xs = (jnp.swapaxes(A11, 0, 1), jnp.swapaxes(A12, 0, 1), jnp.swapaxes(beta, 0, 1), jnp.swapaxes(Kh, 0, 1), jnp.swapaxes(Vg, 0, 1))
            S0 = jnp.zeros((b, H, HD, 2), x.dtype)
            _, Y = jax.lax.scan(step, S0, xs)
            Y = jnp.moveaxis(Y, 0, 1)
            y = jnp.sum(Q * Y, -1).reshape(b, s, DI)
            yg = y.transpose(0, 2, 1).reshape(b, G, DI // G, s)
            mu = jnp.mean(yg, (2, 3), keepdims=True)
            var = jnp.var(yg, (2, 3), keepdims=True)
            yg = (yg - mu) * jax.lax.rsqrt(var + 1e-05)
            y = (yg.reshape(b, DI, s) * gn_w[None, :, None] + gn_b[None, :, None]).transpose(0, 2, 1)
            y = y * jax.nn.silu(z)
            y = y + D * u
            return residual + y @ out_W.T
        return _forward(x, in_proj_W, in_proj_b, conv_w, conv_b, dyn_W, dyn_b, dt_c, selB_W, selC_W, seldt_W, beta_W, beta_b, rg_W, rg_b, ug_W, ug_b, Q_W, out_W, D, rms_w, gn_w, gn_b)

    def _L0_ffn_ref(x, Wr, W1, b1, W2, b2):
        import jax, jax.numpy as jnp
        import numpy as np
        B, T, D, F_FF, E, K = (8, 512, 256, 1024, 8, 2)
        pooled = x.mean(axis=1)
        logits = pooled @ Wr
        top_scores, top_idx = jax.lax.top_k(logits, K)
        weights = jax.nn.softmax(top_scores, axis=-1)
        W1s, b1s = (W1[top_idx], b1[top_idx])
        W2s, b2s = (W2[top_idx], b2[top_idx])
        h = jnp.einsum('btd,bkdf->bktf', x, W1s) + b1s[:, :, None, :]
        h = jax.nn.gelu(h, approximate=False)
        y = jnp.einsum('bktf,bkfd->bktd', h, W2s) + b2s[:, :, None, :]
        out = jnp.einsum('bk,bktd->btd', weights, y)
        return out
    x = L0_attn_x
    x = x + _layernorm(_L0_attn_ref(_layernorm(x, axis=-1), L0_attn_in_proj_W, L0_attn_in_proj_b, L0_attn_conv_w, L0_attn_conv_b, L0_attn_dyn_W, L0_attn_dyn_b, L0_attn_dt_c, L0_attn_selB_W, L0_attn_selC_W, L0_attn_seldt_W, L0_attn_beta_W, L0_attn_beta_b, L0_attn_rg_W, L0_attn_rg_b, L0_attn_ug_W, L0_attn_ug_b, L0_attn_Q_W, L0_attn_out_W, L0_attn_D, L0_attn_rms_w, L0_attn_gn_w, L0_attn_gn_b), axis=-1)
    x = x + _layernorm(_L0_ffn_ref(_layernorm(x, axis=-1), L0_ffn_Wr, L0_ffn_W1, L0_ffn_b1, L0_ffn_W2, L0_ffn_b2), axis=-1)
    return x

_drawn_inputs = setup_inputs


def setup_inputs(seed=0):
    import zlib

    import numpy as np

    out = dict(_drawn_inputs(seed))
    spreads = {'L0_attn_in_proj_b': (0.0, 0.1),
     'L0_attn_conv_b': (0.0, 0.1),
     'L0_attn_dyn_b': (0.0, 0.1),
     'L0_attn_dt_c': (0.5, 0.2),
     'L0_attn_beta_b': (0.0, 0.1),
     'L0_attn_rg_b': (1.0, 0.2),
     'L0_attn_ug_b': (-1.0, 0.2),
     'L0_attn_D': (0.0, 0.1),
     'L0_attn_rms_w': (1.0, 0.2),
     'L0_attn_gn_w': (1.0, 0.2),
     'L0_attn_gn_b': (0.0, 0.1)}
    factors = {}
    for name, (base, spread) in spreads.items():
        noise = np.random.default_rng([zlib.crc32(name.encode()), seed]).standard_normal(out[name].shape)
        drawn = base * np.exp(spread * noise) if base else spread * noise
        out[name] = jnp.asarray(drawn.astype(out[name].dtype))
    for name, factor in factors.items():
        out[name] = (out[name] * factor).astype(out[name].dtype)
    return out
```

```python
from contextlib import ExitStack

import concourse.bass as bass
from concourse import mybir

F32 = mybir.dt.float32
U32 = mybir.dt.uint32
ALU = mybir.AluOpType
ACT = mybir.ActivationFunctionType
AX = mybir.AxisListType

P = 128
B, S, DM, DI, H, HD = 2, 2048, 256, 512, 32, 16
L = S // P
KM, KI = DM // P, DI // P
NCH = S // 512
NSM = 11
E, FF = 8, 1024
FT = FF // P
NV = KI * NCH
NF = NCH * 2 * FT
C_CW, C_CB, C_BV, C_BZ, C_D, C_GW, C_GB, C_RMS = 0, 16, 20, 24, 28, 32, 36, 40
NCOL = 42


def build(nc, x, wv, wz, wk, wq, wsm, wo, cols, bk_row, bsm_row, dtc_row, rope, ident_d, group_d,
          wr, w1, b1, w2, b2, out):
    with ExitStack() as ctx:
        def sb(name, shape, dt=F32):
            return ctx.enter_context(nc.sbuf_tensor(name, shape, dt))

        def sem(name):
            return ctx.enter_context(nc.semaphore(name))

        kap = sb("kap", [P, L * 1024])
        uT = sb("uT", [P, KI * S])
        xnT = sb("xnT", [P, KM, S])
        wshare = sb("wshare", [P, 4096])
        wz_s = sb("wz_s", [P, KM, DI])
        wk_s = sb("wk_s", [P, KM, 2, DI])
        wo_s = sb("wo_s", [P, KI, DM])
        coef = sb("coef", [P, 11 * 512])
        work = sb("work", [P, 7680])
        col = sb("col", [P, NCOL])
        bk_s = sb("bk_s", [1, 2 * DI])
        bsm_s = sb("bsm_s", [P, NSM * H])
        dtc_s = sb("dtc_s", [P, H])
        ident = sb("ident", [P, P])
        group = sb("group", [P, P])
        onerow = sb("onerow", [1, P])
        endf = sb("endf", [P, 12 * H])
        small = sb("small", [P, 576])
        wr_s = sb("wr_s", [P, KM, E])
        idx = sb("idx", [1, 8], U32)
        ps = ctx.enter_context(nc.psum_tensor("ps", [P, 8, 512], F32))

        kap4 = kap[:].rearrange("p (j i n) -> p j i n", j=L, i=2)
        VB = 19 * P
        vbuf = [kap[:, i * VB:(i + 1) * VB].rearrange("p (j c) -> p j c", c=P) for i in range(2)]
        cacc = [kap[:, 2 * VB + i * S:2 * VB + (i + 1) * S] for i in range(2)]
        sall = kap[:, 2 * VB + 2 * S:2 * VB + 2 * S + L * NSM * H].rearrange(
            "p (j q h) -> p q j h", j=L, q=NSM)
        sall_j = kap[:, 2 * VB + 2 * S:2 * VB + 2 * S + L * NSM * H].rearrange("p (j n) -> p j n", j=L)
        uT3 = uT[:].rearrange("p (g t) -> p g t", g=KI)
        x_in = uT[:, 0:L * DM].rearrange("p (j d) -> p j d", j=L)
        x_c = uT[:, L * DM:2 * L * DM].rearrange("p (j d) -> p j d", j=L)
        x_re = coef[:, 0:L * DM].rearrange("p (j d) -> p j d", j=L)
        wv_s = wshare[:, 0:KM * DI].rearrange("p (k n) -> p k n", k=KM)
        wsm_s = wshare[:, KM * DI:KM * DI + KI * NSM * H].rearrange("p (k n) -> p k n", k=KI)
        wq_s = wshare[:, :].rearrange("p (k i n) -> p k i n", k=KI, i=2)
        w1_s = uT[:, 0:4096].rearrange("p (e k n) -> p e k n", e=2, k=KM)
        w2_s = uT[:, 4096:8192].rearrange("p (e f n) -> p e f n", e=2, f=FT)
        cf = coef[:].rearrange("p (q j h) -> p q j h", q=11, j=L)
        G_, H_, RHO, CV, CVS = 0, 4, 8, 9, 10
        r_tok = kap4[:, :, 1, 0:DM]
        x1_tok = kap4[:, :, 0, 0:DM]
        PSt = work[:, 0:3072].rearrange("p (a c n) -> p a c n", a=2, c=3)
        tmp = work[:, 3072:7680]
        mt = work[:, 0:3072].rearrange("p (c o g i) -> p c o g i", o=2, g=KI, i=3)
        st6 = small[:, 0:96].rearrange("p (j s) -> p j s", s=6)
        mv = small[:, 96:128].rearrange("p (j s) -> p j s", s=2)
        mean1, rs1 = small[:, 128:144], small[:, 144:160]
        t0, t1, t2 = small[:, 160:176], small[:, 176:192], small[:, 192:208]
        gst6 = small[:, 208:304].rearrange("p (g n s) -> p g n s", g=KI, n=NCH)
        gmv = small[:, 304:312].rearrange("p (g s) -> p g s", s=2)
        gq = small[:, 312:320].rearrange("p (g s) -> p g s", s=2)
        gA, gB, gt = small[:, 320:324], small[:, 324:328], small[:, 328:332]
        gsb = small[:, 332:340].rearrange("p (g s) -> p g s", s=2)
        pool_j = small[:, 340:372].rearrange("p (k j) -> p k j", k=KM)
        pooled = small[:, 372:374]
        lg, mx8, wrow, wbc = small[0:1, 376:384], small[0:1, 384:392], small[0:1, 392:396], small[:, 396:398]
        eps5, eps6 = small[:, 398:399], small[:, 399:400]
        b1_s = small[:, 400:416].rearrange("p (e f) -> p e f", e=2)
        spc = small[:, 416:448]
        sp_t = small[:, 448:480]
        rs2, m2 = small[:, 480:496], small[:, 496:512]
        one_c = small[:, 512:513]

        x_loaded = sem("x_loaded")
        xr_loaded = sem("xr_loaded")
        wa_loaded = sem("wa_loaded")
        wq_loaded = sem("wq_loaded")
        ex_loaded = sem("ex_loaded")
        out_stored = sem("out_stored")
        xc_ready = sem("xc_ready")
        xt_ready = sem("xt_ready")
        xt_done = sem("xt_done")
        v_ready = sem("v_ready")
        v_done = sem("v_done")
        conv_done = sem("conv_done")
        u_ready = sem("u_ready")
        sm_ready = sem("sm_ready")
        sm_done = sem("sm_done")
        hd_vec = sem("hd_vec")
        hd_act = sem("hd_act")
        st_vec = sem("st_vec")
        st_act = sem("st_act")
        rope_loaded = sem("rope_loaded")
        kq_ready = sem("kq_ready")
        kq_used = sem("kq_used")
        ut_ready = sem("ut_ready")
        ut_used = sem("ut_used")
        end_ready = sem("end_ready")
        end_turned = sem("end_turned")
        mt_ready = sem("mt_ready")
        scan_done = sem("scan_done")
        start_ready = sem("start_ready")
        start_used = sem("start_used")
        y_ready = sem("y_ready")
        yt_ready = sem("yt_ready")
        yt_done = sem("yt_done")
        gq_ready = sem("gq_ready")
        gsum_ready = sem("gsum_ready")
        z_ready = sem("z_ready")
        sz_ready = sem("sz_ready")
        y2_ready = sem("y2_ready")
        o_ready = sem("o_ready")
        o_used = sem("o_used")
        x2_ready = sem("x2_ready")
        x2t_ready = sem("x2t_ready")
        x2t_done = sem("x2t_done")
        pooled_ready = sem("pooled_ready")
        logit_ready = sem("logit_ready")
        idx_ready = sem("idx_ready")
        wrow_ready = sem("wrow_ready")
        wb_ready = sem("wb_ready")
        w2s_ready = sem("w2s_ready")
        h_ready = sem("h_ready")
        h_done = sem("h_done")
        f_ready = sem("f_ready")
        f_used = sem("f_used")
        out_ready = sem("out_ready")
        consts_loaded = sem("consts_loaded")
        const_ready = sem("const_ready")
        vec_chain = sem("vec_chain")
        act_chain = sem("act_chain")

        def ybuf(j):
            return tmp[:, 4096:4608] if j % 2 else work[:, 2560:3072]

        def szb(i):
            return work[:, (i % 2) * 512:(i % 2 + 1) * 512]

        def y2(n):
            return work[:, 2048 + (n % 2) * 2048:2048 + (n % 2 + 1) * 2048].rearrange("p (g t) -> p g t", g=KI)

        def hbuf(i):
            return work[:, (i % 4) * 512:(i % 4 + 1) * 512]

        def HS(n):
            return work[:, n * 512:(n + 1) * 512].rearrange("p (j h) -> p j h", j=L)

        block = ctx.enter_context(nc.Block())

        @block.sync
        def _(sp):
            def load(dst, src):
                sp.dma_start(dst, src).then_inc(consts_loaded, 16)

            def load_x(b):
                if b > 0:
                    sp.wait_ge(f_ready, b * L)
                sp.dma_start(x_in, x[b].rearrange("(c j) d -> c j d", j=L)).then_inc(x_loaded, 16)

            def load_wa(b):
                if b > 0:
                    sp.wait_ge(kq_ready, b * 2 * L)
                sp.dma_start(wv_s, wv.rearrange("(k p) n -> p k n", p=P)).then_inc(wa_loaded, 16)
                sp.dma_start(wsm_s, wsm.rearrange("(k p) n -> p k n", p=P)).then_inc(wa_loaded, 16)

            load_x(0)
            load(ident[:], ident_d[:])
            load(col[:], cols[:])
            load_wa(0)
            load(wk_s[:], wk.rearrange("(k p) i n -> p k i n", p=P))
            load(bk_s[:], bk_row[:])
            load(bsm_s[:], bsm_row.to_broadcast([P, NSM * H]))
            load(dtc_s[:], dtc_row.to_broadcast([P, H]))
            load(wz_s[:], wz.rearrange("(k p) n -> p k n", p=P))
            load(wo_s[:], wo.rearrange("(k p) n -> p k n", p=P))
            load(wr_s[:], wr.rearrange("(k p) n -> p k n", p=P))
            load(group[:], group_d[:])
            for b in range(B):
                if b > 0:
                    load_x(b)
                    load_wa(b)
                if b > 0:
                    sp.wait_ge(f_ready, b * L)
                sp.dma_start(HS(14), rope[:]).then_inc(rope_loaded, 16)
                sp.wait_ge(sm_ready, b * L + L)
                sp.dma_start(wq_s, wq.rearrange("(k p) i n -> p k i n", p=P)).then_inc(wq_loaded, 16)
                sp.wait_ge(y_ready, b * L + L)
                sp.dma_start(x_re, x[b].rearrange("(c j) d -> c j d", j=L)).then_inc(xr_loaded, 16)
                sp.wait_ge(idx_ready, b + 1)
                for e in range(2):
                    ex = sp.value_load(idx[0:1, e:e + 1], min_val=0, max_val=E - 1)
                    sp.dma_start(w1_s[:, e], w1[bass.ds(ex, 1)].rearrange("e (k p) n -> p (e k) n", p=P)
                                 ).then_inc(ex_loaded, 16)
                    sp.dma_start(w2_s[:, e], w2[bass.ds(ex, 1)].rearrange("e (f p) n -> p (e f) n", p=P)
                                 ).then_inc(ex_loaded, 16)
                    sp.dma_start(b1_s[:, e], b1[bass.ds(ex, 1)].rearrange("e p f -> p (e f)")
                                 ).then_inc(ex_loaded, 16)
                    sp.dma_start(coef[:, 4096 + e * DM:4096 + (e + 1) * DM],
                                 b2[bass.ds(ex, 1)].to_broadcast([P, DM])).then_inc(ex_loaded, 16)
                sp.wait_ge(out_ready, b + 1)
                sp.dma_start(out[b].rearrange("(c j) d -> c j d", j=L), x1_tok).then_inc(out_stored, 16)
            sp.wait_ge(out_stored, 16 * B)

        @block.tensor
        def _(pe):
            mm, tr = nc.tensor.matmul, nc.tensor.transpose

            def normed_x(b):
                for j in range(L):
                    pe.wait_ge(xc_ready, b * L + j + 1)
                    if j >= 2:
                        pe.wait_ge(xt_done, b * L + j - 1)
                    for k in range(KM):
                        t = tr(ps[:, 4 + j % 2, k * P:(k + 1) * P], x_c[:, j, k * P:(k + 1) * P], ident[:])
                    t.then_inc(xt_ready, 1)

            def values(b):
                pe.wait_ge(wa_loaded, b * 32 + 32)
                pe.wait_ge(xt_done, b * L + L)
                for i in range(KI * NCH):
                    g, n = i // NCH, i % NCH
                    if i >= 4:
                        pe.wait_ge(v_done, b * NV + i - 3)
                    for k in range(KM):
                        t = mm(ps[:, i % 4, :], wv_s[:, k, g * P:(g + 1) * P], xnT[:, k, n * 512:(n + 1) * 512],
                               start=(k == 0), stop=(k == KM - 1))
                    t.then_inc(v_ready, 1)

            def head_projections(b):
                pe.wait_ge(u_ready, b * KI + KI)
                for j in range(L):
                    if j >= 2:
                        pe.wait_ge(sm_done, b * L + j - 1)
                    for k in range(KI):
                        t = mm(ps[:, 6 + j % 2, 0:NSM * H], uT3[:, k, j * P:(j + 1) * P], wsm_s[:, k, :],
                               start=(k == 0), stop=(k == KI - 1))
                    t.then_inc(sm_ready, 1)

            def token_u(b, i, j):
                if i >= 2:
                    pe.wait_ge(ut_used, 2 * L * b + i - 1)
                for g in range(KI):
                    t = tr(ps[:, 4 + i % 2, g * P:(g + 1) * P], uT3[:, g, j * P:(j + 1) * P], ident[:])
                t.then_inc(ut_ready, 1)

            def keys(b):
                pe.wait_ge(v_done, b * NV + KI * NCH)
                for i in range(L):
                    j = L - 1 - i
                    if i >= 2:
                        pe.wait_ge(kq_used, 2 * L * b + i - 1)
                    for c in range(2):
                        o = ps[:, 2 * (i % 2) + c, :]
                        for k in range(KM):
                            mm(o, xnT[:, k, j * P:(j + 1) * P], wk_s[:, k, c, :], start=(k == 0), stop=False)
                        t = mm(o, onerow[:], bk_s[:, c * DI:(c + 1) * DI], start=False, stop=True)
                    t.then_inc(kq_ready, 1)
                    token_u(b, i, j)

            def turn_ends(b):
                pe.wait_ge(kq_used, 2 * L * b + L)
                pe.wait_ge(ut_used, 2 * L * b + L)
                for o in range(2):
                    pe.wait_ge(end_ready, b * 2 + o + 1)
                    for c in range(3):
                        for g in range(KI):
                            t = tr(ps[:, 3 * o + c, g * P:(g + 1) * P],
                                   tmp[:, 3072 + c * 512 + g * P:3072 + c * 512 + (g + 1) * P], ident[:])
                    t.then_inc(end_turned, 1)

            def turn_starts(b):
                pe.wait_ge(scan_done, b + 1)
                hist = tmp[:, 0:129 * 12].rearrange("p (c g i) -> p i g c", g=KI, i=3)
                for o in range(2):
                    for g in range(KI):
                        t = tr(ps[:, 6 + o, g * P:(g + 1) * P], hist[:, o, g, 0:P], ident[:])
                t.then_inc(start_ready, 1)

            def turn_y(b, j):
                pe.wait_ge(y_ready, b * L + j + 1)
                if j >= 2:
                    pe.wait_ge(yt_done, b * L + j - 1)
                else:
                    pe.wait_ge(start_used, b + 1)
                for g in range(KI):
                    t = tr(ps[:, 6 + j % 2, g * P:(g + 1) * P], ybuf(j)[:, g * P:(g + 1) * P], ident[:])
                t.then_inc(yt_ready, 1)

            def queries(b):
                pe.wait_ge(wq_loaded, b * 16 + 16)
                pe.wait_ge(mt_ready, b * 2 + 2)
                for j in range(L):
                    if j >= 2:
                        pe.wait_ge(kq_used, 2 * L * b + L + j - 1)
                    for c in range(2):
                        for k in range(KI):
                            t = mm(ps[:, 2 * (j % 2) + c, :], uT3[:, k, j * P:(j + 1) * P], wq_s[:, k, c, :],
                                   start=(k == 0), stop=(k == KI - 1))
                    t.then_inc(kq_ready, 1)
                    token_u(b, L + j, j)
                    if j == 0:
                        turn_starts(b)
                    if j >= 1:
                        turn_y(b, j - 1)
                turn_y(b, L - 1)

            def group_sums(b):
                pe.wait_ge(yt_done, b * L + L)
                pe.wait_ge(gq_ready, b + 1)
                mm(ps[:, 6, 0:8], group[:], gq.rearrange("p g s -> p (g s)"),
                   start=True, stop=True).then_inc(gsum_ready, 1)

            def gates_and_output(b):
                pe.wait_ge(kq_used, 2 * L * b + 2 * L)
                pe.wait_ge(ut_used, 2 * L * b + 2 * L)

                def z(n):
                    for g in range(KI):
                        i = n * KI + g
                        if i >= 4:
                            pe.wait_ge(sz_ready, b * NV + i - 3)
                        for k in range(KM):
                            t = mm(ps[:, i % 4, :], wz_s[:, k, g * P:(g + 1) * P],
                                   xnT[:, k, n * 512:(n + 1) * 512], start=(k == 0), stop=(k == KM - 1))
                        t.then_inc(z_ready, 1)

                z(0)
                for n in range(NCH):
                    if n + 1 < NCH:
                        z(n + 1)
                    pe.wait_ge(y2_ready, b * NV + (n + 1) * KI)
                    for q in range(4):
                        j = 4 * n + q
                        if j >= 2:
                            pe.wait_ge(o_used, b * L + j - 1)
                        for g in range(KI):
                            t = mm(ps[:, 4 + j % 2, 0:DM], y2(n)[:, g, q * P:(q + 1) * P], wo_s[:, g, :],
                                   start=(g == 0), stop=(g == KI - 1))
                        t.then_inc(o_ready, 1)

            def turn_x2(b):
                for j in range(L):
                    pe.wait_ge(x2_ready, b * L + j + 1)
                    if j >= 2:
                        pe.wait_ge(x2t_done, b * L + j - 1)
                    for k in range(KM):
                        t = tr(ps[:, 6 + j % 2, k * P:(k + 1) * P], r_tok[:, j, k * P:(k + 1) * P], ident[:])
                    t.then_inc(x2t_ready, 1)

            def router(b):
                pe.wait_ge(x2t_done, b * L + L)
                pe.wait_ge(pooled_ready, b + 1)
                for k in range(KM):
                    t = mm(ps[0:1, 6, 0:E], pooled[:, k:k + 1], wr_s[:, k, :], start=(k == 0), stop=(k == KM - 1))
                t.then_inc(logit_ready, 1)
                pe.wait_ge(wrow_ready, b + 1)
                mm(ps[:, 7, 0:2], onerow[:], wrow[:, 0:2], start=True, stop=True).then_inc(wb_ready, 1)

            def experts(b):
                pe.wait_ge(ex_loaded, b * 128 + 128)
                pe.wait_ge(w2s_ready, b + 1)

                def up(n, f):
                    i = n * 2 * FT + f
                    if i >= 4:
                        pe.wait_ge(h_done, b * NF + i - 3)
                    for k in range(KM):
                        t = mm(ps[:, i % 4, :], w1_s[:, f // FT, k, (f % FT) * P:(f % FT + 1) * P],
                               xnT[:, k, n * 512:(n + 1) * 512], start=(k == 0), stop=(k == KM - 1))
                    t.then_inc(h_ready, 1)

                def down(n, f):
                    i = n * 2 * FT + f
                    pe.wait_ge(h_done, b * NF + i + 1)
                    for q in range(4):
                        if f == 0 and n > 0:
                            pe.wait_ge(f_used, b * L + 4 * (n - 1) + q + 1)
                        t = mm(ps[:, 4 + q, 0:DM], hbuf(i)[:, q * P:(q + 1) * P], w2_s[:, f // FT, f % FT, :],
                               start=(f == 0), stop=(f == 2 * FT - 1))
                        if f == 2 * FT - 1:
                            t.then_inc(f_ready, 1)

                for i in range(NCH * 2 * FT + 2):
                    if i < NCH * 2 * FT:
                        up(i // (2 * FT), i % (2 * FT))
                    if i >= 2:
                        down((i - 2) // (2 * FT), (i - 2) % (2 * FT))

            pe.wait_ge(consts_loaded, 16 * 10)
            pe.wait_ge(const_ready, 1)
            for b in range(B):
                normed_x(b)
                values(b)
                head_projections(b)
                keys(b)
                turn_ends(b)
                queries(b)
                group_sums(b)
                gates_and_output(b)
                turn_x2(b)
                router(b)
                experts(b)

        @block.scalar
        def _(act):
            n_chain = [0]
            af = nc.scalar.activation

            def link(ins):
                n_chain[0] += 1
                ins.then_inc(act_chain, 1)
                act.wait_ge(act_chain, n_chain[0])

            def root(b, k, dst, src, eps):
                act.wait_ge(st_vec, b * 6 + k)
                af(dst, src, ACT.Sqrt, bias=eps).then_inc(st_act, 1)

            def normed_x(b):
                root(b, 1, t1, mv[:, :, 1], eps5)
                root(b, 2, t1, t0, eps6)
                for j in range(L):
                    act.wait_ge(xt_ready, b * L + j + 1)
                    for k in range(KM):
                        t = af(xnT[:, k, j * P:(j + 1) * P], ps[:, 4 + j % 2, k * P:(k + 1) * P], ACT.Copy,
                               scale=col[:, C_RMS + k:C_RMS + k + 1])
                    t.then_inc(xt_done, 1)

            def values_and_u(b):
                if b > 0:
                    act.wait_ge(out_stored, 16 * b)
                for g in range(KI + 1):
                    if g < KI:
                        if g >= 2:
                            act.wait_ge(conv_done, b * KI + g - 1)
                        for n in range(NCH):
                            i = g * NCH + n
                            act.wait_ge(v_ready, b * NV + i + 1)
                            af(vbuf[g % 2][:, 3 + 4 * n:7 + 4 * n, :],
                               ps[:, i % 4, :].rearrange("p (j c) -> p j c", c=P),
                               ACT.Identity, bias=col[:, C_BV + g:C_BV + g + 1]).then_inc(v_done, 1)
                    if g >= 1:
                        act.wait_ge(conv_done, b * KI + g)
                        af(uT3[:, g - 1, :], cacc[(g - 1) % 2], ACT.Silu).then_inc(u_ready, 1)

            def heads(b):
                act.wait_ge(hd_vec, b * 5 + 1)
                for t, src in ((HS(0), sall[:, 0]), (HS(1), sall[:, 3]), (sp_t, dtc_s[:])):
                    link(af(t, src, ACT.Abs))
                    link(af(t, t, ACT.Exp, scale=-1.0))
                    af(t, t, ACT.Ln, bias=one_c).then_inc(hd_act, 1)
                af(sall[:, 8:11], sall[:, 8:11], ACT.Sigmoid).then_inc(hd_act, 1)
                act.wait_ge(hd_vec, b * 5 + 2)
                af(HS(4), HS(3), ACT.Abs).then_inc(hd_act, 1)
                act.wait_ge(hd_vec, b * 5 + 3)
                af(HS(9), HS(9), ACT.Ln).then_inc(hd_act, 1)
                act.wait_ge(hd_vec, b * 5 + 4)
                af(HS(9), HS(9), ACT.Tanh, scale=0.5).then_inc(hd_act, 1)
                act.wait_ge(hd_vec, b * 5 + 5)
                af(work[:, 12 * 512:15 * 512], work[:, 9 * 512:12 * 512], ACT.Sqrt).then_inc(hd_act, 1)

            def passes(b):
                act.wait_ge(end_turned, b * 2 + 2)
                for o in range(2):
                    for i in range(3):
                        t = af(mt[:, :, o, :, i].rearrange("p c g -> p g c"),
                               ps[:, 3 * o + i, :].rearrange("p (g c) -> p g c", g=KI), ACT.Copy)
                    t.then_inc(mt_ready, 1)
                for j in range(L):
                    act.wait_ge(yt_ready, b * L + j + 1)
                    af(kap4[:, j, 0, :], ps[:, 6 + j % 2, :], ACT.Copy).then_inc(yt_done, 1)

            def gates_and_norms(b):
                root(b, 3, gt, gt, eps5)
                for i in range(KI * NCH):
                    g = i % KI
                    act.wait_ge(z_ready, b * NV + i + 1)
                    if i >= 2:
                        act.wait_ge(y2_ready, b * NV + i - 1)
                    af(szb(i), ps[:, i % 4, :], ACT.Silu, bias=col[:, C_BZ + g:C_BZ + g + 1]
                       ).then_inc(sz_ready, 1)
                root(b, 4, t1, mv[:, :, 1], eps5)
                root(b, 5, t1, mv[:, :, 1], eps5)
                for j in range(L):
                    act.wait_ge(x2t_ready, b * L + j + 1)
                    for k in range(KM):
                        t = af(xnT[:, k, j * P:(j + 1) * P], ps[:, 6 + j % 2, k * P:(k + 1) * P], ACT.Identity,
                               accum_out=pool_j[:, k, j:j + 1])
                    t.then_inc(x2t_done, 1)

            def experts(b):
                act.wait_ge(idx_ready, b + 1)
                af(wrow[:, 2:3], wrow[:, 3:4], ACT.Exp).then_inc(st_act, 1)
                act.wait_ge(ex_loaded, b * 128 + 128)
                for i in range(NCH * 2 * FT):
                    f = i % (2 * FT)
                    act.wait_ge(h_ready, b * NF + i + 1)
                    af(hbuf(i), ps[:, i % 4, :], ACT.Gelu, bias=b1_s[:, f // FT, f % FT:f % FT + 1]
                       ).then_inc(h_done, 1)
                root(b, 6, t1, mv[:, :, 1], eps5)

            act.wait_ge(consts_loaded, 16 * 10)
            act.wait_ge(const_ready, 1)
            for b in range(B):
                normed_x(b)
                values_and_u(b)
                heads(b)
                passes(b)
                gates_and_norms(b)
                experts(b)

        @block.vector
        def _(dve):
            n_chain = [0]
            v = nc.vector

            def link(ins):
                n_chain[0] += 1
                ins.then_inc(vec_chain, 1)
                dve.wait_ge(vec_chain, n_chain[0])

            tt, tsc = v.tensor_tensor, v.tensor_scalar

            def stt(o, a, s1, c, op0, op1):
                return v.scalar_tensor_tensor(out=o, in0=a, scalar=s1, in1=c, op0=op0, op1=op1)

            MUL, ADD, SUB, MAX = ALU.mult, ALU.add, ALU.subtract, ALU.max

            def stats(j, src):
                link(v.bn_stats(st6[:, j, :], src))
                link(v.bn_aggr(mv[:, j, :], st6[:, j, :]))

            def inverse_std(b, k):
                v.tensor_copy(m2, mv[:, :, 0]).then_inc(st_vec, 1)
                dve.wait_ge(st_vec, b * 6 + (k if k < 6 else 6))
                dve.wait_ge(st_act, b * 7 + k)
                link(v.reciprocal(rs2, t1))

            def normed_x(b):
                dve.wait_ge(x_loaded, b * 16 + 16)
                for j in range(L):
                    stats(j, x_in[:, j, :])
                v.tensor_copy(mean1, mv[:, :, 0]).then_inc(st_vec, 1)
                dve.wait_ge(st_vec, b * 6 + 1)
                dve.wait_ge(st_act, b * 7 + 1)
                link(v.reciprocal(rs1, t1))
                link(tt(t0, rs1, rs1, MUL))
                tt(t0, t0, mv[:, :, 1], MUL).then_inc(st_vec, 1)
                dve.wait_ge(st_vec, b * 6 + 2)
                dve.wait_ge(st_act, b * 7 + 2)
                link(v.reciprocal(t2, t1))
                link(tt(t2, t2, rs1, MUL))
                for j in range(L):
                    tsc(x_c[:, j, :], x_in[:, j, :], mean1[:, j:j + 1], t2[:, j:j + 1], SUB, MUL).then_inc(xc_ready, 1)
                    dve.wait_ge(xc_ready, b * L + j + 1)

            def convolution(b):
                for g in range(KI):
                    dve.wait_ge(v_done, b * NV + (g + 1) * NCH)
                    V, acc = vbuf[g % 2], cacc[g % 2].rearrange("p (j c) -> p j c", c=P)
                    if g >= 2:
                        dve.wait_ge(u_ready, b * KI + g - 1)
                    link(v.memset(V[:, 0:3, 0:1], 0.0))
                    link(v.tensor_copy(V[:, 0:3, 1:P], V[:, L:L + 3, 0:P - 1]))
                    w = lambda k: col[:, C_CW + 4 * g + k:C_CW + 4 * g + k + 1]
                    link(tsc(acc, V[:, 3:19, :], w(3), col[:, C_CB + g:C_CB + g + 1], MUL, ADD))
                    for k in (2, 1):
                        link(stt(acc, V[:, k:k + L, :], w(k), acc, MUL, ADD))
                    stt(acc, V[:, 0:L, :], w(0), acc, MUL, ADD).then_inc(conv_done, 1)
                    dve.wait_ge(conv_done, b * KI + g + 1)

            def heads(b):
                for j in range(L):
                    dve.wait_ge(sm_ready, b * L + j + 1)
                    tt(sall_j[:, j, :], ps[:, 6 + j % 2, 0:NSM * H], bsm_s[:], ADD).then_inc(sm_done, 1)
                    dve.wait_ge(sm_done, b * L + j + 1)
                tt(HS(2), sall[:, 1], sall[:, 2], ADD).then_inc(hd_vec, 1)
                dve.wait_ge(hd_vec, b * 5 + 1)
                dve.wait_ge(rope_loaded, b * 16 + 16)
                tt(HS(3), HS(2), HS(14), ADD).then_inc(hd_vec, 1)
                dve.wait_ge(hd_vec, b * 5 + 2)
                dve.wait_ge(hd_act, b * 8 + 3)
                link(stt(HS(0), sall[:, 0], 0.0, HS(0), MAX, ADD))
                link(stt(HS(1), sall[:, 3], 0.0, HS(1), MAX, ADD))
                link(stt(spc, dtc_s[:], 0.0, sp_t, MAX, ADD))
                dve.wait_ge(hd_act, b * 8 + 4)
                dve.wait_ge(hd_act, b * 8 + 5)
                link(stt(HS(5), HS(4), 1e-4, HS(0), ADD, ADD))
                link(v.reciprocal(HS(5), HS(5)))
                link(tt(HS(5), HS(5), spc.unsqueeze(1).to_broadcast([P, L, H]), MUL))
                link(tt(HS(5), HS(5), HS(1), ADD))
                link(stt(HS(6), HS(5), 0.5, HS(0), MUL, MUL))
                link(stt(HS(7), HS(5), 0.5, HS(3), MUL, MUL))
                link(tt(HS(8), HS(6), HS(6), MUL))
                link(tt(HS(2), HS(7), HS(7), MUL))
                link(tsc(HS(4), HS(6), 1.0, None, ADD))
                link(tt(HS(4), HS(4), HS(4), MUL))
                link(tt(HS(4), HS(4), HS(2), ADD))
                link(v.reciprocal(HS(4), HS(4)))
                link(tsc(HS(5), HS(6), -1.0, None, ADD))
                link(tt(HS(5), HS(5), HS(5), MUL))
                link(tt(HS(5), HS(5), HS(2), ADD))
                link(tt(HS(9), HS(5), HS(4), MUL))
                tsc(HS(9), HS(9), 1e-19, None, MAX).then_inc(hd_vec, 1)
                dve.wait_ge(hd_vec, b * 5 + 3)
                link(tt(HS(8), HS(8), HS(2), ADD))
                link(tsc(HS(8), HS(8), -1.0, 1.0, MUL, ADD))
                link(tt(HS(0), HS(8), HS(4), MUL))
                link(tsc(HS(0), HS(0), 1e-16, None, ADD))
                link(stt(HS(1), HS(7), 2.0, HS(4), MUL, MUL))
                link(tt(HS(10), HS(0), HS(0), MUL))
                link(tt(HS(3), HS(1), HS(1), MUL))
                link(tt(HS(10), HS(10), HS(3), ADD))
                link(v.tensor_copy(HS(11), sall[:, 8]))
                dve.wait_ge(hd_act, b * 8 + 6)
                tt(HS(9), HS(9), sall[:, 9], MUL).then_inc(hd_vec, 1)
                dve.wait_ge(hd_vec, b * 5 + 4)
                dve.wait_ge(hd_act, b * 8 + 7)
                link(tsc(HS(4), HS(9), -1.0, 1.0, MUL, ADD))
                link(v.reciprocal(HS(4), HS(4)))
                link(stt(HS(9), HS(9), -2.0, HS(4), MUL, MUL))
                tsc(HS(9), HS(9), 1e-6, None, MAX).then_inc(hd_vec, 1)
                dve.wait_ge(hd_vec, b * 5 + 5)
                dve.wait_ge(hd_act, b * 8 + 8)
                vp, rho, sbeta = HS(12), HS(13), HS(14)
                link(v.reciprocal(HS(5), rho))
                link(tt(HS(10), HS(10), HS(5), MUL))
                link(tt(HS(10), HS(10), rho, ADD))
                link(tsc(rho, HS(10), 0.5, None, MUL))
                link(tt(HS(10), rho, HS(5), MUL))
                link(tsc(HS(10), HS(10), -1.0, 2.0, MUL, ADD))
                link(tt(HS(5), HS(5), HS(10), MUL))
                link(v.tensor_copy(cf[:, RHO], rho))
                link(tt(HS(2), vp, sbeta, MUL))
                link(tt(cf[:, CV], HS(2), sall[:, 10], MUL))
                link(tt(HS(0), HS(0), HS(5), MUL))
                link(tt(HS(1), HS(1), HS(5), MUL))
                link(v.tensor_copy(work[:, 3072:3584 + 512].rearrange("p (q j h) -> p q j h", q=2, j=L)[:, :, 0], work[:, 0:1024].rearrange("p (q j h) -> p q j h", q=2, j=L)[:, :, 0]))
                for j in range(1, L):
                    o = work[:, 3072:4096].rearrange("p (q j h) -> p q j h", q=2, j=L)
                    prod = work[:, 1024:1088].rearrange("p (q h) -> p q h", q=2)
                    link(tt(prod, o[:, :, j - 1], HS(0)[:, j:j + 1].to_broadcast([P, 2, H]), MUL))
                    link(tt(HS(3)[:, 0], o[:, 1, j - 1], HS(1)[:, j], MUL))
                    link(tt(HS(3)[:, 1], o[:, 0, j - 1], HS(1)[:, j], MUL))
                    link(tt(o[:, 0, j], prod[:, 0], HS(3)[:, 0], SUB))
                    link(tt(o[:, 1, j], prod[:, 1], HS(3)[:, 1], ADD))
                C, Sn = HS(6), HS(7)
                link(v.memset(HS(8)[:, L - 1], 1.0))
                for j in range(L - 1, 0, -1):
                    link(tt(HS(8)[:, j - 1], HS(8)[:, j], rho[:, j], MUL))
                link(tt(cf[:, CVS], cf[:, CV], HS(8), MUL))
                link(tt(HS(5)[:, 0], HS(8)[:, 0], rho[:, 0], MUL))
                link(tt(HS(2), sbeta, sall[:, 4], MUL))
                link(tt(HS(3), sbeta, sall[:, 5], MUL))
                link(tt(cf[:, G_ + 0], C, HS(2), MUL))
                link(stt(cf[:, G_ + 1], Sn, -1.0, HS(3), MUL, MUL))
                link(tt(cf[:, G_ + 2], Sn, HS(2), MUL))
                link(tt(cf[:, G_ + 3], C, HS(3), MUL))
                link(tt(cf[:, H_ + 0], C, sall[:, 6], MUL))
                link(tt(cf[:, H_ + 1], Sn, sall[:, 6], MUL))
                link(stt(cf[:, H_ + 2], Sn, -1.0, sall[:, 7], MUL, MUL))
                link(tt(cf[:, H_ + 3], C, sall[:, 7], MUL))
                ef = endf[:].rearrange("p (q c h) -> p q c h", q=4, c=3)
                link(v.tensor_copy(ef[:, 0, 2], C[:, L - 1]))
                link(v.tensor_copy(ef[:, 3, 2], C[:, L - 1]))
                link(v.tensor_copy(ef[:, 1, 2], Sn[:, L - 1]))
                link(tsc(ef[:, 2, 2], Sn[:, L - 1], -1.0, None, MUL))
                for c in range(2):
                    link(tt(ef[:, :, c], ef[:, :, 2], HS(5)[:, 0:1].to_broadcast([P, 4, H]), MUL))

            def by_head(ap, n):
                return ap.rearrange("p i (h d) -> p i h d", h=H) if n else ap.rearrange("p (h d) -> p h d", h=H)

            def wide(ap):
                return ap.unsqueeze(len(ap.shape)).to_broadcast([*ap.shape, HD])

            def pass_1(b):
                link(v.memset(work[:, 0:3072], 0.0))
                link(v.memset(PSt[:, 0, 0], 1.0))
                link(v.memset(PSt[:, 1, 1], 1.0))
                X = tmp[:, 0:2048].rearrange("p (a i n) -> p a i n", a=2, i=2)
                g = tmp[:, 2048:3072].rearrange("p (a n) -> p a n", a=2)
                vs = tmp[:, 3072:3584]
                Z = tmp[:, 3584:4608].rearrange("p (a n) -> p a n", a=2)
                for i in range(L):
                    j = L - 1 - i
                    k = kap4[:, j]
                    K = ps[:, 2 * (i % 2):2 * (i % 2) + 2, :]
                    dve.wait_ge(kq_ready, 2 * L * b + i + 1)
                    link(tt(by_head(X[:, 0], 1), by_head(K, 1), wide(cf[:, G_:G_ + 2, j]), MUL))
                    tt(by_head(X[:, 1], 1), by_head(K, 1), wide(cf[:, G_ + 2:G_ + 4, j]), MUL).then_inc(kq_used, 1)
                    dve.wait_ge(kq_used, 2 * L * b + i + 1)
                    link(tt(k, X[:, :, 0], X[:, :, 1], ADD))
                    dve.wait_ge(ut_ready, 2 * L * b + i + 1)
                    tt(by_head(vs, 0), by_head(ps[:, 4 + i % 2, :], 0), wide(cf[:, CVS, j]), MUL).then_inc(ut_used, 1)
                    dve.wait_ge(ut_used, 2 * L * b + i + 1)
                    kb = k.unsqueeze(1).to_broadcast([P, 2, 2, DI])
                    link(tt(X, PSt[:, :, 0:2], kb, MUL))
                    link(tt(g, X[:, :, 0], X[:, :, 1], ADD))
                    link(tt(Z, g, vs.unsqueeze(1).to_broadcast([P, 2, DI]), MUL))
                    link(tt(PSt[:, :, 2], PSt[:, :, 2], Z, ADD))
                    link(tt(X, g.unsqueeze(2).to_broadcast([P, 2, 2, DI]), kb, MUL))
                    link(tt(PSt[:, :, 0:2], PSt[:, :, 0:2], X, SUB))

            def chunk_scan(b):
                ef = endf[:].rearrange("p (o a c h) -> p o a c h", o=2, a=2, c=3)
                X = tmp[:, 0:3072].rearrange("p (a c n) -> p a c n", a=2, c=3)
                M = tmp[:, 3072:4608].rearrange("p (c n) -> p c n", c=3)
                for o in range(2):
                    for a in range(2):
                        link(tt(by_head(X[:, a], 1), by_head(PSt[:, a], 1), wide(ef[:, o, a]), MUL))
                    if o:
                        dve.wait_ge(end_turned, b * 2 + 1)
                    tt(M, X[:, 0], X[:, 1], ADD).then_inc(end_ready, 1)
                    dve.wait_ge(end_ready, b * 2 + o + 1)
                hist = tmp[:, 0:129 * 12].rearrange("p (c g i) -> p c g i", g=KI, i=3)
                prod = tmp[:, 1600:1624].rearrange("p (o g i) -> p o g i", o=2, g=KI)
                link(v.memset(hist, 1.0))
                link(v.memset(hist[:, 0, :, 0:2], 0.0))
                dve.wait_ge(mt_ready, b * 2 + 2)
                for c in range(P - 1):
                    link(tt(prod, mt[:, c], hist[:, c].unsqueeze(1).to_broadcast([P, 2, KI, 3]), MUL))
                    link(v.tensor_reduce(hist[:, c + 1, :, 0:2].rearrange("p g o -> p o g"), prod, AX.X, ADD))
                v.tensor_copy(hist[:, 0, :, 2], hist[:, 1, :, 2]).then_inc(scan_done, 1)
                dve.wait_ge(scan_done, b + 1)

            def pass_2(b):
                st = work[:, 0:1024].rearrange("p (i n) -> p i n", i=2)
                sr = work[:, 1024:2048].rearrange("p (i n) -> p i n", i=2)
                Y = tmp[:, 0:1024].rearrange("p (i n) -> p i n", i=2)
                e, vh = tmp[:, 1024:1536], tmp[:, 1536:2048]
                X = tmp[:, 2048:4096].rearrange("p (a i n) -> p a i n", a=2, i=2)
                Z = tmp[:, 2048:3072].rearrange("p (i n) -> p i n", i=2)
                dve.wait_ge(start_ready, b + 1)
                v.tensor_copy(st, ps[:, 6:8, :]).then_inc(start_used, 1)
                dve.wait_ge(start_used, b + 1)
                for j in range(L):
                    k = kap4[:, j]
                    for i in range(2):
                        link(tt(by_head(sr[:, i], 0), by_head(st[:, i], 0), wide(cf[:, RHO, j]), MUL))
                    link(tt(Y, k, sr, MUL))
                    link(tt(e, Y[:, 0], Y[:, 1], ADD))
                    dve.wait_ge(ut_ready, 2 * L * b + L + j + 1)
                    tt(by_head(vh, 0), by_head(ps[:, 4 + j % 2, :], 0), wide(cf[:, CV, j]), MUL).then_inc(ut_used, 1)
                    dve.wait_ge(ut_used, 2 * L * b + L + j + 1)
                    link(tt(e, vh, e, SUB))
                    link(tt(Y, k, e.unsqueeze(1).to_broadcast([P, 2, DI]), MUL))
                    link(tt(st, sr, Y, ADD))
                    for i in range(2):
                        link(tt(by_head(X[:, i], 1), by_head(st, 1), wide(cf[:, H_ + 2 * i:H_ + 2 * i + 2, j]), MUL))
                    link(tt(Y, X[:, :, 0], X[:, :, 1], ADD))
                    dve.wait_ge(kq_ready, 2 * L * b + L + j + 1)
                    tt(Z, Y, ps[:, 2 * (j % 2):2 * (j % 2) + 2, :], MUL).then_inc(kq_used, 1)
                    dve.wait_ge(kq_used, 2 * L * b + L + j + 1)
                    if j >= 2:
                        dve.wait_ge(yt_ready, b * L + j - 1)
                    tt(ybuf(j), Z[:, 0], Z[:, 1], ADD).then_inc(y_ready, 1)
                    dve.wait_ge(y_ready, b * L + j + 1)
                    if j % 4 == 1 and j > 4:
                        group_stats(b, j // 4 - 1)
                group_stats(b, NCH - 1)

            def group_stats(b, n):
                dve.wait_ge(yt_done, b * L + 4 * n + 4)
                for g in range(KI):
                    link(v.bn_stats(gst6[:, g, n, :], kap4[:, 4 * n:4 * n + 4, 0, g * P:(g + 1) * P]))

            def group_norm(b):
                for g in range(KI):
                    link(v.bn_aggr(gmv[:, g, :], gst6[:, g].rearrange("p n s -> p (n s)")))
                link(v.tensor_copy(gq[:, :, 0], gmv[:, :, 0]))
                link(tt(gq[:, :, 1], gmv[:, :, 0], gmv[:, :, 0], MUL))
                tt(gq[:, :, 1], gq[:, :, 1], gmv[:, :, 1], ADD).then_inc(gq_ready, 1)
                dve.wait_ge(gq_ready, b + 1)
                dve.wait_ge(gsum_ready, b + 1)
                link(v.tensor_copy(gsb, ps[:, 6, 0:8].rearrange("p (g s) -> p g s", s=2)))
                link(tt(gt, gsb[:, :, 0], gsb[:, :, 0], MUL))
                tt(gt, gsb[:, :, 1], gt, SUB).then_inc(st_vec, 1)
                dve.wait_ge(st_vec, b * 6 + 3)
                dve.wait_ge(st_act, b * 7 + 3)
                link(v.reciprocal(gA, gt))
                link(tt(gA, gA, col[:, C_GW:C_GW + KI], MUL))
                link(tt(gB, gsb[:, :, 0], gA, MUL))
                link(tt(gB, col[:, C_GB:C_GB + KI], gB, SUB))

            def residual(b, n):
                for j in range(4 * n, 4 * n + 4):
                    link(tsc(r_tok[:, j], x_re[:, j], mean1[:, j:j + 1], rs1[:, j:j + 1], SUB, MUL))
                    dve.wait_ge(o_ready, b * L + j + 1)
                    tt(r_tok[:, j], r_tok[:, j], ps[:, 4 + j % 2, 0:DM], ADD).then_inc(o_used, 1)
                    dve.wait_ge(o_used, b * L + j + 1)
                    stats(j, r_tok[:, j])

            def gates_and_norms(b):
                dve.wait_ge(xr_loaded, b * 16 + 16)
                for n in range(NCH):
                    for g in range(KI):
                        i = n * KI + g
                        ty = work[:, 1024 + (i % 2) * 512:1536 + (i % 2) * 512]
                        link(tsc(ty.rearrange("p (j c) -> p j c", c=P), kap4[:, 4 * n:4 * n + 4, 0, g * P:(g + 1) * P], gA[:, g:g + 1], gB[:, g:g + 1], MUL, ADD))
                        dve.wait_ge(sz_ready, b * NV + i + 1)
                        link(tt(ty, ty, szb(i), MUL))
                        if n >= 2:
                            dve.wait_ge(o_ready, b * L + 4 * (n - 1))
                        stt(y2(n)[:, g, :], uT3[:, g, n * 512:(n + 1) * 512], col[:, C_D + g:C_D + g + 1], ty, MUL, ADD).then_inc(y2_ready, 1)
                        dve.wait_ge(y2_ready, b * NV + i + 1)
                    if n >= 1:
                        residual(b, n - 1)
                residual(b, NCH - 1)
                inverse_std(b, 4)
                for j in range(L):
                    link(tsc(r_tok[:, j], r_tok[:, j], m2[:, j:j + 1], rs2[:, j:j + 1], SUB, MUL))
                    link(tt(x1_tok[:, j], r_tok[:, j], x_re[:, j], ADD))
                    stats(j, x1_tok[:, j])
                inverse_std(b, 5)
                for j in range(L):
                    tsc(r_tok[:, j], x1_tok[:, j], m2[:, j:j + 1], rs2[:, j:j + 1], SUB, MUL).then_inc(x2_ready, 1)
                    dve.wait_ge(x2_ready, b * L + j + 1)

            def router(b):
                dve.wait_ge(x2t_done, b * L + L)
                link(v.tensor_reduce(pooled, pool_j, AX.X, ADD))
                tsc(pooled, pooled, 1.0 / S, None, MUL).then_inc(pooled_ready, 1)
                dve.wait_ge(pooled_ready, b + 1)
                dve.wait_ge(logit_ready, b + 1)
                link(v.tensor_copy(lg, ps[0:1, 6, 0:E]))
                link(v.max(mx8, lg))
                link(v.max_index(idx[:], mx8, lg))
                tt(wrow[:, 3:4], mx8[:, 1:2], mx8[:, 0:1], SUB).then_inc(idx_ready, 1)
                dve.wait_ge(idx_ready, b + 1)
                dve.wait_ge(st_act, b * 7 + 6)
                link(tsc(wrow[:, 1:2], wrow[:, 2:3], 1.0, None, ADD))
                link(v.reciprocal(wrow[:, 0:1], wrow[:, 1:2]))
                tt(wrow[:, 1:2], wrow[:, 0:1], wrow[:, 2:3], MUL).then_inc(wrow_ready, 1)
                dve.wait_ge(wrow_ready, b + 1)
                dve.wait_ge(wb_ready, b + 1)
                link(v.tensor_copy(wbc, ps[:, 7, 0:2]))
                dve.wait_ge(ex_loaded, b * 128 + 128)
                b2c = coef[:, 4096:4096 + DM]
                link(tsc(b2c, b2c, wbc[:, 0:1], None, MUL))
                link(stt(b2c, coef[:, 4096 + DM:4096 + 2 * DM], wbc[:, 1:2], b2c, MUL, ADD))
                link(tsc(w2_s[:, 0], w2_s[:, 0], wbc[:, 0:1], None, MUL))
                tsc(w2_s[:, 1], w2_s[:, 1], wbc[:, 1:2], None, MUL).then_inc(w2s_ready, 1)
                dve.wait_ge(w2s_ready, b + 1)

            def experts(b):
                b2c = coef[:, 4096:4096 + DM]
                for j in range(L):
                    dve.wait_ge(f_ready, b * L + j + 1)
                    tt(r_tok[:, j], ps[:, 4 + j % 4, 0:DM], b2c, ADD).then_inc(f_used, 1)
                    dve.wait_ge(f_used, b * L + j + 1)
                    stats(j, r_tok[:, j])
                inverse_std(b, 7)
                for j in range(L):
                    link(tsc(r_tok[:, j], r_tok[:, j], m2[:, j:j + 1], rs2[:, j:j + 1], SUB, MUL))
                    if j < L - 1:
                        link(tt(x1_tok[:, j], r_tok[:, j], x1_tok[:, j], ADD))
                tt(x1_tok[:, L - 1], r_tok[:, L - 1], x1_tok[:, L - 1], ADD).then_inc(out_ready, 1)
                dve.wait_ge(out_ready, b + 1)

            link(v.memset(eps5, 1e-5))
            link(v.memset(eps6, 1e-6))
            link(v.memset(one_c, 1.0))
            v.memset(onerow[:], 1.0).then_inc(const_ready, 1)
            dve.wait_ge(const_ready, 1)
            dve.wait_ge(consts_loaded, 16 * 10)
            for b in range(B):
                normed_x(b)
                convolution(b)
                heads(b)
                pass_1(b)
                chunk_scan(b)
                pass_2(b)
                group_norm(b)
                gates_and_norms(b)
                router(b)
                experts(b)


def program(nc, arrays):
    def dram(name, a):
        return nc.dram_tensor(f"in_{name}", a.shape, F32, kind="ExternalInput").ap()

    args = {name: dram(name, a) for name, a in arrays.items()}
    out = nc.dram_tensor("out", (B, S, DM), F32, kind="ExternalOutput").ap()
    build(nc, **args, out=out)


def kernel(**inputs):
    import numpy as np
    import concourse.bacc as bacc
    from concourse.bass_utils import run_bass_kernel_spmd

    t = {k.replace("L0_attn_", "a_").replace("L0_ffn_", "f_"): np.asarray(v) for k, v in inputs.items()}
    W, bias = t["a_in_proj_W"], t["a_in_proj_b"]

    def by_component(w):
        return np.moveaxis(w.reshape(-1, 2, w.shape[-1]), 1, 0)

    def tiles(v):
        return v.reshape(-1, P).T

    cw = t["a_conv_w"].reshape(KI, P, 4).transpose(1, 0, 2).reshape(P, 16)
    dyn, dynb = t["a_dyn_W"], t["a_dyn_b"]
    sb_, sc_ = by_component(t["a_selB_W"]), by_component(t["a_selC_W"])
    wsm = np.concatenate([dyn, t["a_seldt_W"], sb_[0], sb_[1], sc_[0], sc_[1], t["a_beta_W"], t["a_rg_W"],
                          t["a_ug_W"]], 0).T
    bsm = np.concatenate([dynb, np.zeros(5 * H, np.float32), t["a_beta_b"], t["a_rg_b"], t["a_ug_b"]])
    freq = (np.float32(1.0) / np.float32(10000.0) ** (np.arange(H, dtype=np.float32) / np.float32(H))).astype(np.float32)
    pos = np.arange(S, dtype=np.float32).reshape(P, L)
    arrays = dict(
        x=t["a_x"],
        wv=W[3 * DI:].T, wz=W[:DI].T,
        wk=by_component(W[DI:3 * DI]).transpose(2, 0, 1), wq=by_component(t["a_Q_W"]).transpose(2, 0, 1),
        wsm=wsm, wo=t["a_out_W"].T,
        cols=np.concatenate([cw, tiles(t["a_conv_b"]), tiles(bias[3 * DI:]), tiles(bias[:DI]), tiles(t["a_D"]),
                             tiles(t["a_gn_w"]), tiles(t["a_gn_b"]), tiles(t["a_rms_w"])], 1),
        bk_row=bias[DI:3 * DI].reshape(DI, 2).T.reshape(1, -1), bsm_row=bsm.reshape(1, -1),
        dtc_row=t["a_dt_c"].reshape(1, -1), rope=(pos[:, :, None] * freq).astype(np.float32),
        ident_d=np.eye(P, dtype=np.float32),
        group_d=np.kron(np.eye(P // HD, dtype=np.float32), np.full((HD, HD), 1.0 / HD, np.float32)),
        wr=t["f_Wr"], w1=t["f_W1"], b1=t["f_b1"].reshape(E, FT, P).transpose(0, 2, 1), w2=t["f_W2"], b2=t["f_b2"])
    arrays = {k: np.ascontiguousarray(v) for k, v in arrays.items()}
    nc = bacc.Bacc("TRN2", target_bir_lowering=False, num_devices=1)
    program(nc, arrays)
    r = run_bass_kernel_spmd(nc, [{f"in_{k}": v for k, v in arrays.items()}], core_ids=[0])
    return r.results[0]["out"]
```
